# Optimizing a Trainium2 kernel written in Bass

```python
import numpy as np
import jax
import jax.numpy as jnp

def _softmax(x, axis=-1):
    return jax.nn.softmax(x, axis=axis)

def _gelu(x):
    return jax.nn.gelu(x, approximate=True)

def _silu(x):
    return jax.nn.silu(x)

def _sigmoid(x):
    return jax.nn.sigmoid(x)

def _layernorm(x, axis=-1, eps=1e-05):
    m = jnp.mean(x, axis=axis, keepdims=True)
    v = jnp.var(x, axis=axis, keepdims=True)
    return (x - m) / jnp.sqrt(v + eps)

def _scatter_add(tgt, idx, src, axis=0):
    return tgt.at[idx].add(src)

def _segment_sum(src, seg, n):
    return jax.ops.segment_sum(src, seg, n)
kernel_name = 'mk_rec_standalone_d1_rec_r8_3430cf'

def setup_inputs(seed: int=0):
    np.random.seed(seed)
    _w = jnp.asarray

    def _rec_inputs():
        import jax
        import jax.numpy as jnp
        _rk = jax.random.key(seed)
        r_state = -0.000928989 + 1.00043 * jax.random.normal(jax.random.fold_in(_rk, 1), (1024, 256), jnp.float32)
        r_token = jax.random.randint(jax.random.fold_in(_rk, 2), (1024,), 49, 31986, jnp.int32)
        return (r_state, r_token)
    r_state, r_token = _rec_inputs()

    def _L0_rec_setup():
        import jax, jax.numpy as jnp
        import numpy as np
        VOCAB = 4000
        HIDDEN = 256
        NLAYERS = 6
        BATCH = 512
        key = jax.random.key(seed)
        k1, k2, k3, k4 = jax.random.split(key, 4)
        state = jax.random.normal(k1, (BATCH, HIDDEN), dtype=jnp.float32)
        token = jax.random.randint(k2, (BATCH,), 0, VOCAB, dtype=jnp.int32)
        ih = jax.random.normal(k3, (NLAYERS, VOCAB, HIDDEN), dtype=jnp.float32) * 0.02
        hh = jax.random.normal(k4, (NLAYERS, HIDDEN, HIDDEN), dtype=jnp.float32) * 0.02
        return {'state': state, 'token': token, 'ih': ih, 'hh': hh}
    _L0_rec_all = _L0_rec_setup()
    _L0_rec_in = {k: v for k, v in _L0_rec_all.items() if k in ('ih', 'hh')}
    del _L0_rec_all
    return {'r_state': r_state, 'r_token': r_token, 'L0_rec_ih': _L0_rec_in['ih'], 'L0_rec_hh': _L0_rec_in['hh']}

def reference(r_state, r_token, L0_rec_ih, L0_rec_hh):
    import jax
    import jax.numpy as jnp

    def _L0_rec_ref(state, token, ih, hh):
        import jax, jax.numpy as jnp
        import numpy as np
        VOCAB = 4000
        HIDDEN = 256
        NLAYERS = 6
        BATCH = 512
        n_layers = ih.shape[0]
        for i in range(n_layers):
            gate = ih[i][token]
            state = jnp.tanh(state + jnp.matmul(state, hh[i]) * gate)
        return state
    y = _L0_rec_ref(r_state, r_token, L0_rec_ih, L0_rec_hh)
    return y

_drawn_inputs = setup_inputs


def setup_inputs(seed=0):
    import zlib

    import numpy as np

    out = dict(_drawn_inputs(seed))
    spreads = {}
    factors = {'L0_rec_ih': 3.854, 'L0_rec_hh': 3.835}
    for name, (base, spread) in spreads.items():
        noise = np.random.default_rng([zlib.crc32(name.encode()), seed]).standard_normal(out[name].shape)
        drawn = base * np.exp(spread * noise) if base else spread * noise
        out[name] = jnp.asarray(drawn.astype(out[name].dtype))
    for name, factor in factors.items():
        out[name] = (out[name] * factor).astype(out[name].dtype)
    return out
```

```python
import concourse.bass as bass
from concourse import mybir
from contextlib import ExitStack

P = 128
BATCH = 1024
HIDDEN = 256
LAYERS = 6
VOCAB = 4000
KC = HIDDEN // P
QUARTERS = 4
QB = BATCH // QUARTERS
TILES = BATCH // P
TPQ = TILES // QUARTERS
PARTS = 2
LAYERS_PER_ROW = LAYERS // PARTS
ROW = LAYERS_PER_ROW * HIDDEN
STEPS = LAYERS * QUARTERS
LAST = STEPS - QUARTERS
GATE_BANKS = 4

TURN_ORDER = [l * QUARTERS + q for q in range(QUARTERS) for l in (0, 1)] + list(range(2 * QUARTERS, STEPS))
TURN_OF = {s: k for k, s in enumerate(TURN_ORDER)}
POOL_LOW = []
POOL_WEIGHTS = [3, 4, 5]


def recurrent_cells(nc, state_t, token, gates, hh, out_t):
    f32, f32r = mybir.dt.float32, mybir.dt.float32r
    i32, u32 = mybir.dt.int32, mybir.dt.uint32
    ALU, ACT = mybir.AluOpType, mybir.ActivationFunctionType

    gate_rows = gates.rearrange("v (h r) -> (v h) r", h=PARTS)
    state_v = state_t.rearrange("(c p) (q b) -> q p c b", p=P, q=QUARTERS)
    out_v = out_t.rearrange("(c p) (q b) -> q p c b", p=P, q=QUARTERS)
    w_v = hh.rearrange("l (c p) n -> l p c n", p=P)

    with ExitStack() as ctx:
        def sb(name, shape, dt):
            return ctx.enter_context(nc.sbuf_tensor(name, shape, dt))

        def sem(name):
            return ctx.enter_context(nc.semaphore(name))

        tok = sb("tok", [P, TILES], i32)
        tok_c = sb("tok_c", [P, TILES], f32)
        wrap = sb("wrap", [P, TILES], f32)
        tok_f = sb("tok_f", [P, TILES], f32)
        row_of = sb("row_of", [P, PARTS, TILES], i32)
        gate = sb("gate", [P, PARTS, TILES, ROW], f32)
        gate_t = sb("gate_t", [P, STEPS, KC, QB], f32)
        w = sb("w", [P, LAYERS, KC, HIDDEN], f32)
        wh = sb("wh", [P, LAYERS, KC, HIDDEN], f32r)
        wl = sb("wl", [P, LAYERS, KC, HIDDEN], f32r)
        s = sb("s", [P, QUARTERS, KC, QB], f32)
        sh = sb("sh", [P, QUARTERS, KC, QB], f32r)
        sl = sb("sl", [P, QUARTERS, KC, QB], f32r)
        pre = sb("pre", [P, QUARTERS, KC, QB], f32)
        ident = sb("ident", [P, P], f32)
        prod = [ctx.enter_context(nc.psum_tensor(f"prod{q}", [P, KC, QB], f32)) for q in range(QUARTERS)]
        turned = [ctx.enter_context(nc.psum_tensor(f"turned{b}", [P, KC, QB], f32)) for b in range(GATE_BANKS)]

        tok_in = sem("tok_in")
        state_in = [sem(f"state_in{q}") for q in range(QUARTERS)]
        w_in = [sem(f"w_in{l}") for l in range(LAYERS)]
        gate_in = [[sem(f"gate_in{h}_{t}") for t in range(TILES)] for h in range(PARTS)]
        ident_zero = sem("ident_zero")
        ident_ready = sem("ident_ready")
        index_step = sem("index_step")
        rows_ready = sem("rows_ready")
        wh_ready = sem("wh_ready")
        wl_dve = sem("wl_dve")
        wl_pool = sem("wl_pool")
        sh_ready = sem("sh_ready")
        sl_dve = sem("sl_dve")
        sl_pool = sem("sl_pool")
        s_ready = sem("s_ready")
        gate_turned = sem("gate_turned")
        gate_ready = sem("gate_ready")
        prod_ready = sem("prod_ready")
        gated = sem("gated")
        pre_ready = sem("pre_ready")
        out_done = sem("out_done")

        def wait_wl(eng, l):
            if l in POOL_WEIGHTS:
                eng.wait_ge(wl_pool, POOL_WEIGHTS.index(l) + 1)
            else:
                eng.wait_ge(wl_dve, sum(k not in POOL_WEIGHTS for k in range(l + 1)))

        def wait_sl(eng, n):
            made = n - QUARTERS
            if made in POOL_LOW:
                eng.wait_ge(sl_pool, POOL_LOW.index(made) + 1)
            else:
                eng.wait_ge(sl_dve, n + 1 - sum(k <= made for k in POOL_LOW))

        with nc.Block() as block:

            @block.sync
            def _(sp):
                sp.dma_start(tok[:, :], token).then_inc(tok_in, 16)
                sp.dma_start(s[:, 0], state_v[0]).then_inc(state_in[0], 16)
                sp.dma_start(w[:, 0], w_v[0]).then_inc(w_in[0], 16)
                for q in range(1, QUARTERS):
                    sp.dma_start(s[:, q], state_v[q]).then_inc(state_in[q], 16)
                sp.dma_start(w[:, 1], w_v[1]).then_inc(w_in[1], 16)
                for l in range(2, LAYERS):
                    sp.wait_ge(gate_in[0][min(TILES - 1, 2 * l + 1)], 16)
                    sp.dma_start(w[:, l], w_v[l]).then_inc(w_in[l], 16)
                for q in range(QUARTERS):
                    sp.wait_ge(s_ready, LAST + q + 1)
                    sp.dma_start(out_v[q], s[:, q]).then_inc(out_done, 16)
                sp.wait_ge(out_done, 16 * QUARTERS)

            @block.gpsimd
            def _(pool):
                nc.gpsimd.memset(ident[:, :], 0.0).then_inc(ident_zero, 1)
                pool.wait_ge(ident_zero, 1)
                nc.gpsimd.affine_select(out=ident[:, :], in_=ident[:, :], compare_op=ALU.not_equal, fill=1.0,
                                        base=0, pattern=[[-1, P]], channel_multiplier=1).then_inc(ident_ready, 1)
                for h in range(PARTS):
                    pool.wait_ge(rows_ready, h + 1)
                    for t in range(TILES):
                        nc.gpsimd.indirect_dma_start(
                            gate[:, h, t], None, gate_rows,
                            bass.IndirectOffsetOnAxis(row_of[:, h, t:t + 1].bitcast(u32), 0),
                        ).then_inc(gate_in[h][t], 16)
                for l in POOL_WEIGHTS:
                    pool.wait_ge(w_in[l], 16)
                    pool.wait_ge(wh_ready, l + 1)
                    nc.gpsimd.tensor_tensor(wl[:, l], w[:, l], wh[:, l].bitcast(f32), ALU.subtract).then_inc(wl_pool, 1)
                for n in POOL_LOW:
                    q = n % QUARTERS
                    pool.wait_ge(s_ready, n + 1)
                    nc.gpsimd.tensor_tensor(sl[:, q], s[:, q], sh[:, q].bitcast(f32), ALU.subtract).then_inc(sl_pool, 1)

            @block.scalar
            def _(act):
                def round_weights(l):
                    act.wait_ge(w_in[l], 16)
                    nc.scalar.copy(wh[:, l], w[:, l]).then_inc(wh_ready, 1)

                def round_input(q):
                    act.wait_ge(state_in[q], 16)
                    nc.scalar.copy(sh[:, q], s[:, q]).then_inc(sh_ready, 1)

                def keep_gates(n):
                    k = TURN_OF[n]
                    act.wait_ge(gate_turned, k + 1)
                    nc.scalar.copy(gate_t[:, n], turned[k % GATE_BANKS][:, :, :]).then_inc(gate_ready, 1)

                def tanh(n):
                    q = n % QUARTERS
                    act.wait_ge(pre_ready, n + 1)
                    if n < LAST:
                        nc.scalar.activation(sh[:, q], pre[:, q], ACT.Tanh).then_inc(sh_ready, 1)
                    nc.scalar.activation(s[:, q], pre[:, q], ACT.Tanh).then_inc(s_ready, 1)

                round_input(0)
                round_weights(0)
                for q in range(1, QUARTERS):
                    round_input(q)
                round_weights(1)
                for n in TURN_ORDER[0:4]:
                    keep_gates(n)
                for q in range(QUARTERS):
                    tanh(q)
                    for n in TURN_ORDER[4 + 2 * q:6 + 2 * q] if q < 2 else []:
                        keep_gates(n)
                round_weights(2)
                for n in range(QUARTERS, STEPS):
                    tanh(n)
                    if 2 * QUARTERS <= n + 3 < STEPS:
                        keep_gates(n + 3)
                    if n % QUARTERS == 2 and n // QUARTERS + 2 < LAYERS:
                        round_weights(n // QUARTERS + 2)

            @block.vector
            def _(dve):
                dve.wait_ge(tok_in, 16)
                nc.vector.tensor_scalar(tok_c[:, :], tok[:, :], -float(VOCAB), float(VOCAB - 1), ALU.max, ALU.min).then_inc(index_step, 1)
                dve.wait_ge(index_step, 1)
                nc.vector.tensor_scalar(wrap[:, :], tok_c[:, :], 0.0, float(VOCAB), ALU.is_lt, ALU.mult).then_inc(index_step, 1)
                dve.wait_ge(index_step, 2)
                nc.vector.tensor_tensor(tok_f[:, :], tok_c[:, :], wrap[:, :], ALU.add).then_inc(index_step, 1)
                dve.wait_ge(index_step, 3)
                for h in range(PARTS):
                    nc.vector.tensor_scalar(row_of[:, h], tok_f[:, :], float(PARTS), float(h), ALU.mult, ALU.add).then_inc(rows_ready, 1)

                def low_weights(l):
                    dve.wait_ge(w_in[l], 16)
                    dve.wait_ge(wh_ready, l + 1)
                    nc.vector.tensor_tensor(wl[:, l], w[:, l], wh[:, l].bitcast(f32), ALU.subtract).then_inc(wl_dve, 1)

                def low_state(q):
                    nc.vector.tensor_tensor(sl[:, q], s[:, q], sh[:, q].bitcast(f32), ALU.subtract).then_inc(sl_dve, 1)

                def low_input(q):
                    dve.wait_ge(state_in[q], 16)
                    dve.wait_ge(sh_ready, q + 1)
                    low_state(q)

                low_input(0)
                low_weights(0)
                for q in range(1, QUARTERS):
                    low_input(q)
                low_weights(1)
                for n in range(STEPS):
                    q = n % QUARTERS
                    dve.wait_ge(prod_ready, n + 1)
                    dve.wait_ge(gate_ready, TURN_OF[n] + 1)
                    nc.vector.tensor_tensor(pre[:, q], prod[q][:, :, :], gate_t[:, n], ALU.mult).then_inc(gated, 1)
                    dve.wait_ge(gated, n + 1)
                    nc.vector.tensor_tensor(pre[:, q], pre[:, q], s[:, q], ALU.add).then_inc(pre_ready, 1)
                    if 0 <= n - 1 < LAST and n - 1 not in POOL_LOW:
                        dve.wait_ge(s_ready, n)
                        low_state((n - 1) % QUARTERS)
                    if n % QUARTERS == 3 and n // QUARTERS + 2 < LAYERS and n // QUARTERS + 2 not in POOL_WEIGHTS:
                        low_weights(n // QUARTERS + 2)

            @block.tensor
            def _(pe):
                def turn(k):
                    n = TURN_ORDER[k]
                    l, q = divmod(n, QUARTERS)
                    h, j = divmod(l, LAYERS_PER_ROW)
                    if k >= GATE_BANKS:
                        pe.wait_ge(gate_ready, k - GATE_BANKS + 1)
                    for t in range(TPQ):
                        tile = q * TPQ + t
                        pe.wait_ge(gate_in[h][tile], 16)
                        for c in range(KC):
                            at = j * HIDDEN + c * P
                            last = nc.tensor.transpose(turned[k % GATE_BANKS][:, c, t * P:(t + 1) * P],
                                                       gate[:, h, tile, at:at + P], ident[:, :])
                    last.then_inc(gate_turned, 1)

                def product(n):
                    l, q = divmod(n, QUARTERS)
                    pe.wait_ge(wh_ready, l + 1)
                    pe.wait_ge(sh_ready, n + 1)
                    for m in range(KC):
                        passes = [(wh, sh), (wl, sh), (wh, sl)]
                        for i, (a, b) in enumerate(passes):
                            if m == 0 and i == 1:
                                wait_wl(pe, l)
                            if m == 0 and i == 2:
                                wait_sl(pe, n)
                            for c in range(KC):
                                last = nc.tensor.matmul(prod[q][:, m, :], a[:, l, c, m * P:(m + 1) * P], b[:, q, c, :],
                                                        start=(i == 0 and c == 0), stop=(i == 2 and c == KC - 1))
                    last.then_inc(prod_ready, 1)

                for n in range(QUARTERS):
                    product(n)
                pe.wait_ge(ident_ready, 1)
                for k in range(4):
                    turn(k)
                for n in range(QUARTERS, STEPS):
                    product(n)
                    if n == 4:
                        turn(4), turn(5)
                    elif n == 5:
                        turn(6), turn(7)
                    elif n + 2 < STEPS:
                        turn(n + 2)


def kernel(r_state, r_token, L0_rec_ih, L0_rec_hh):
    import numpy as _np
    import concourse.bacc as _bacc
    from concourse import mybir as _mybir
    from concourse.bass_utils import run_bass_kernel_spmd as _run

    arrays = {
        "state_t": _np.ascontiguousarray(_np.asarray(r_state).T),
        "token": _np.ascontiguousarray(_np.asarray(r_token).reshape(TILES, P).T),
        "gates": _np.ascontiguousarray(_np.asarray(L0_rec_ih).transpose(1, 0, 2)).reshape(VOCAB, LAYERS * HIDDEN),
        "hh": _np.ascontiguousarray(_np.asarray(L0_rec_hh)),
    }
    nc = _bacc.Bacc("TRN2", target_bir_lowering=False, num_devices=1)
    args = [nc.dram_tensor(f"{n}_dram", a.shape, _mybir.dt.from_np(a.dtype), kind="ExternalInput").ap() for n, a in arrays.items()]
    args.append(nc.dram_tensor("out_t_dram", (HIDDEN, BATCH), _mybir.dt.float32, kind="ExternalOutput").ap())
    recurrent_cells(nc, *args)
    r = _run(nc, [{f"{n}_dram": a for n, a in arrays.items()}], core_ids=[0])
    return _np.ascontiguousarray(r.results[0]["out_t_dram"].T)
```

```python
import concourse.bass as bass
from concourse import mybir
from contextlib import ExitStack

P = 128
BATCH = 1024
HIDDEN = 256
LAYERS = 6
VOCAB = 4000
KC = HIDDEN // P
QUARTERS = 4
QB = BATCH // QUARTERS
TILES = BATCH // P
TPQ = TILES // QUARTERS
PART_LAYERS = [2, 2, 2]
PARTS = len(PART_LAYERS)
FIRST_LAYER = [sum(PART_LAYERS[:h]) for h in range(PARTS)]
STEPS = LAYERS * QUARTERS
LAST = STEPS - QUARTERS
GATE_BANKS = 4
WARM_UP = 18

TURN_ORDER = [0, 1, 2, 4, 3, 5, 6, 7] + list(range(2 * QUARTERS, STEPS))
TURN_OF = {s: k for k, s in enumerate(TURN_ORDER)}
START = [(0, []), (1, [0]), (2, [1]), (3, [2, 4, 3]), (4, [5, 6]), (5, [7]), (6, [8])]
ACT_START = [("gates", 0), ("weights", 1), ("gates", 1), ("tanh", 0), ("gates", 2), ("gates", 4), ("tanh", 1), ("gates", 3), ("tanh", 2), ("weights", 2), ("tanh", 3), ("gates", 5), ("gates", 6), ("tanh", 4), ("gates", 7), ("tanh", 5)]
LOW_LAG = 2
ACT_STARTED = 6
DVE_WEIGHTS = {0: 1, 8: 3, 12: 4, 16: 5}
WEIGHTS_AFTER = {1: (0, 0), 2: (0, 3), 3: (1, 0), 4: (1, 2), 5: (1, 4)}
POOL_LOW = [5, 7, 9, 11, 13, 15, 17, 19]
POOL_GATHERS = {5: [0, 1], 7: [2, 3], 9: [4, 5], 11: [6, 7]}
POOL_WEIGHTS_AFTER = {(1, 5): 2}
POOL_WEIGHTS = [2]


def recurrent_cells(nc, state_t, token, gate_rows, hh, out_t):
    f32, f32r = mybir.dt.float32, mybir.dt.float32r
    i32, u32 = mybir.dt.int32, mybir.dt.uint32
    ALU, ACT = mybir.AluOpType, mybir.ActivationFunctionType

    state_v = state_t.rearrange("(c p) (q b) -> q p c b", p=P, q=QUARTERS)
    out_v = out_t.rearrange("(c p) (q b) -> q p c b", p=P, q=QUARTERS)
    w_v = hh.rearrange("l (c p) n -> l p c n", p=P)

    with ExitStack() as ctx:
        def sb(name, shape, dt):
            return ctx.enter_context(nc.sbuf_tensor(name, shape, dt))

        def sem(name):
            return ctx.enter_context(nc.semaphore(name))

        tok = sb("tok", [P, TILES], i32)
        tok_c = sb("tok_c", [P, TILES], f32)
        wrap = sb("wrap", [P, TILES], f32)
        row_of = sb("row_of", [P, TILES], i32)
        gate = [sb(f"gate{h}", [P, TILES, PART_LAYERS[h] * HIDDEN], f32) for h in range(PARTS)]
        gate_t = sb("gate_t", [P, STEPS, KC, QB], f32)
        w = sb("w", [P, LAYERS, KC, HIDDEN], f32)
        wh = sb("wh", [P, LAYERS, KC, HIDDEN], f32r)
        wl = sb("wl", [P, LAYERS, KC, HIDDEN], f32r)
        s = sb("s", [P, QUARTERS, KC, QB], f32)
        sh = sb("sh", [P, QUARTERS, KC, QB], f32r)
        sl = sb("sl", [P, QUARTERS, KC, QB], f32r)
        pre = sb("pre", [P, QUARTERS, KC, QB], f32)
        ident = sb("ident", [P, P], f32)
        prod = [ctx.enter_context(nc.psum_tensor(f"prod{q}", [P, KC, QB], f32)) for q in range(QUARTERS)]
        turned = [ctx.enter_context(nc.psum_tensor(f"turned{b}", [P, KC, QB], f32)) for b in range(GATE_BANKS)]

        tok_in = sem("tok_in")
        state_in = [sem(f"state_in{q}") for q in range(QUARTERS)]
        w_in = [sem(f"w_in{l}") for l in range(LAYERS)]
        gate_in = [[sem(f"gate_in{h}_{t}") for t in range(TILES)] for h in range(PARTS)]
        ident_zero = sem("ident_zero")
        ident_ready = sem("ident_ready")
        index_step = sem("index_step")
        rows_ready = sem("rows_ready")
        wh_ready = sem("wh_ready")
        wl_dve = sem("wl_dve")
        wl_pool = sem("wl_pool")
        sh_ready = sem("sh_ready")
        sl_dve = sem("sl_dve")
        sl_pool = sem("sl_pool")
        s_ready = sem("s_ready")
        gate_turned = sem("gate_turned")
        gate_ready = sem("gate_ready")
        prod_ready = sem("prod_ready")
        gated = sem("gated")
        pre_ready = sem("pre_ready")
        out_done = sem("out_done")

        def wait_wl(eng, l):
            if l in POOL_WEIGHTS:
                eng.wait_ge(wl_pool, POOL_WEIGHTS.index(l) + 1)
            else:
                eng.wait_ge(wl_dve, sum(k not in POOL_WEIGHTS for k in range(l + 1)))

        def wait_sl(eng, n):
            made = n - QUARTERS
            if made in POOL_LOW:
                eng.wait_ge(sl_pool, POOL_LOW.index(made) + 1)
            else:
                eng.wait_ge(sl_dve, n + 1 - sum(k <= made for k in POOL_LOW))

        with nc.Block() as block:

            @block.sync
            def _(sp):
                def load_state(q):
                    sp.dma_start(s[:, q], state_v[q]).then_inc(state_in[q], 16)

                def load_weights(l):
                    sp.dma_start(w[:, l], w_v[l]).then_inc(w_in[l], 16)

                sp.dma_start(tok[:, :], token).then_inc(tok_in, 16)
                load_state(0)
                load_weights(0)
                load_state(1)
                load_state(2)
                sp.wait_ge(rows_ready, 1)
                load_state(3)
                for l in range(1, LAYERS):
                    h, t = WEIGHTS_AFTER[l]
                    sp.wait_ge(gate_in[h][t], 16)
                    load_weights(l)
                for q in range(QUARTERS):
                    sp.wait_ge(s_ready, LAST + q + 1)
                    sp.dma_start(out_v[q], s[:, q]).then_inc(out_done, 16)
                sp.wait_ge(out_done, 16 * QUARTERS)

            @block.gpsimd
            def _(pool):
                nc.gpsimd.memset(ident[:, :], 0.0).then_inc(ident_zero, 1)
                pool.wait_ge(ident_zero, 1)
                nc.gpsimd.affine_select(out=ident[:, :], in_=ident[:, :], compare_op=ALU.not_equal, fill=1.0,
                                        base=0, pattern=[[-1, P]], channel_multiplier=1).then_inc(ident_ready, 1)
                def gather(h, t):
                    nc.gpsimd.indirect_dma_start(
                        gate[h][:, t], None, gate_rows[h],
                        bass.IndirectOffsetOnAxis(row_of[:, t:t + 1].bitcast(u32), 0),
                    ).then_inc(gate_in[h][t], 16)

                def low_weights(l):
                    pool.wait_ge(w_in[l], 16)
                    pool.wait_ge(wh_ready, l + 1)
                    nc.gpsimd.tensor_tensor(wl[:, l], w[:, l], wh[:, l].bitcast(f32), ALU.subtract).then_inc(wl_pool, 1)

                pool.wait_ge(rows_ready, 1)
                for h in range(PARTS - 1):
                    for t in range(TILES):
                        gather(h, t)
                        if (h, t) in POOL_WEIGHTS_AFTER:
                            low_weights(POOL_WEIGHTS_AFTER[h, t])
                for n in POOL_LOW:
                    q = n % QUARTERS
                    pool.wait_ge(s_ready, n + 1)
                    nc.gpsimd.tensor_tensor(sl[:, q], s[:, q], sh[:, q].bitcast(f32), ALU.subtract).then_inc(sl_pool, 1)
                    for t in POOL_GATHERS.get(n, []):
                        gather(PARTS - 1, t)

            @block.scalar
            def _(act):
                def round_weights(l):
                    act.wait_ge(w_in[l], 16)
                    nc.scalar.copy(wh[:, l], w[:, l]).then_inc(wh_ready, 1)

                def round_input(q):
                    act.wait_ge(state_in[q], 16)
                    nc.scalar.copy(sh[:, q], s[:, q]).then_inc(sh_ready, 1)

                def keep_gates(n):
                    k = TURN_OF[n]
                    act.wait_ge(gate_turned, k + 1)
                    nc.scalar.copy(gate_t[:, n], turned[k % GATE_BANKS][:, :, :]).then_inc(gate_ready, 1)

                def tanh(n):
                    q = n % QUARTERS
                    act.wait_ge(pre_ready, n + 1)
                    if n < LAST:
                        nc.scalar.activation(sh[:, q], pre[:, q], ACT.Tanh).then_inc(sh_ready, 1)
                    nc.scalar.activation(s[:, q], pre[:, q], ACT.Tanh).then_inc(s_ready, 1)

                round_input(0)
                round_weights(0)
                for q in range(1, QUARTERS):
                    round_input(q)
                for kind, k in ACT_START:
                    {"gates": keep_gates, "weights": round_weights, "tanh": tanh}[kind](k)
                keep_gates(8)
                for n in range(ACT_STARTED, STEPS):
                    tanh(n)
                    if n + 3 < STEPS:
                        keep_gates(n + 3)
                    if n % QUARTERS == 2 and 3 <= n // QUARTERS + 2 < LAYERS:
                        round_weights(n // QUARTERS + 2)

            @block.vector
            def _(dve):
                dve.wait_ge(tok_in, 16)
                nc.vector.tensor_scalar(tok_c[:, :], tok[:, :], -float(VOCAB), float(VOCAB - 1), ALU.max, ALU.min).then_inc(index_step, 1)
                dve.wait_ge(index_step, 1)
                nc.vector.tensor_scalar(wrap[:, :], tok_c[:, :], 0.0, float(VOCAB), ALU.is_lt, ALU.mult).then_inc(index_step, 1)
                dve.wait_ge(index_step, 2)
                nc.vector.tensor_tensor(row_of[:, :], tok_c[:, :], wrap[:, :], ALU.add).then_inc(rows_ready, 1)

                def low_weights(l):
                    dve.wait_ge(w_in[l], 16)
                    dve.wait_ge(wh_ready, l + 1)
                    nc.vector.tensor_tensor(wl[:, l], w[:, l], wh[:, l].bitcast(f32), ALU.subtract).then_inc(wl_dve, 1)

                def low_state(q):
                    nc.vector.tensor_tensor(sl[:, q], s[:, q], sh[:, q].bitcast(f32), ALU.subtract).then_inc(sl_dve, 1)

                def low_input(q):
                    dve.wait_ge(state_in[q], 16)
                    dve.wait_ge(sh_ready, q + 1)
                    low_state(q)

                low_input(0)
                low_weights(0)
                for q in range(1, QUARTERS):
                    low_input(q)
                for n in range(STEPS):
                    q = n % QUARTERS
                    dve.wait_ge(prod_ready, n + 1)
                    dve.wait_ge(gate_ready, TURN_OF[n] + 1)
                    nc.vector.tensor_tensor(pre[:, q], prod[q][:, :, :], gate_t[:, n], ALU.mult).then_inc(gated, 1)
                    made = n - LOW_LAG
                    if 0 <= made < LAST and made not in POOL_LOW:
                        dve.wait_ge(s_ready, made + 1)
                        low_state(made % QUARTERS)
                    dve.wait_ge(gated, n + 1)
                    nc.vector.tensor_tensor(pre[:, q], pre[:, q], s[:, q], ALU.add).then_inc(pre_ready, 1)
                    if n in DVE_WEIGHTS:
                        low_weights(DVE_WEIGHTS[n])

            @block.tensor
            def _(pe):
                def turn(k):
                    n = TURN_ORDER[k]
                    l, q = divmod(n, QUARTERS)
                    h = max(h for h in range(PARTS) if FIRST_LAYER[h] <= l)
                    if k >= GATE_BANKS:
                        pe.wait_ge(gate_ready, k - GATE_BANKS + 1)
                    for t in range(TPQ):
                        tile = q * TPQ + t
                        pe.wait_ge(gate_in[h][tile], 16)
                        for c in range(KC):
                            at = (l - FIRST_LAYER[h]) * HIDDEN + c * P
                            last = nc.tensor.transpose(turned[k % GATE_BANKS][:, c, t * P:(t + 1) * P],
                                                       gate[h][:, tile, at:at + P], ident[:, :])
                    last.then_inc(gate_turned, 1)

                def product(n):
                    l, q = divmod(n, QUARTERS)
                    pe.wait_ge(wh_ready, l + 1)
                    pe.wait_ge(sh_ready, n + 1)
                    for m in range(KC):
                        passes = [(wh, sh), (wl, sh), (wh, sl)]
                        for i, (a, b) in enumerate(passes):
                            if m == 0 and i == 1:
                                wait_wl(pe, l)
                            if m == 0 and i == 2:
                                wait_sl(pe, n)
                            for c in range(KC):
                                last = nc.tensor.matmul(prod[q][:, m, :], a[:, l, c, m * P:(m + 1) * P], b[:, q, c, :],
                                                        start=(i == 0 and c == 0), stop=(i == 2 and c == KC - 1))
                    last.then_inc(prod_ready, 1)

                pe.wait_ge(ident_ready, 1)
                for _ in range(WARM_UP):
                    nc.tensor.transpose(turned[0][:, 0, 0:P], ident[:, :], ident[:, :])
                for n, turns in START:
                    product(n)
                    for k in turns:
                        turn(TURN_OF[k])
                for n in range(len(START), STEPS):
                    product(n)
                    if n + 2 < STEPS:
                        turn(n + 2)


def kernel(r_state, r_token, L0_rec_ih, L0_rec_hh):
    import numpy as _np
    import concourse.bacc as _bacc
    from concourse import mybir as _mybir
    from concourse.bass_utils import run_bass_kernel_spmd as _run

    ih = _np.asarray(L0_rec_ih).transpose(1, 0, 2)
    arrays = {
        "state_t": _np.ascontiguousarray(_np.asarray(r_state).T),
        "token": _np.ascontiguousarray(_np.asarray(r_token).reshape(TILES, P).T),
        "hh": _np.ascontiguousarray(_np.asarray(L0_rec_hh)),
    }
    for h, l in enumerate(FIRST_LAYER):
        arrays[f"gates{h}"] = _np.ascontiguousarray(ih[:, l:l + PART_LAYERS[h]]).reshape(VOCAB, -1)
    nc = _bacc.Bacc("TRN2", target_bir_lowering=False, num_devices=1)
    dram = {n: nc.dram_tensor(f"{n}_dram", a.shape, _mybir.dt.from_np(a.dtype), kind="ExternalInput").ap() for n, a in arrays.items()}
    out_t = nc.dram_tensor("out_t_dram", (HIDDEN, BATCH), _mybir.dt.float32, kind="ExternalOutput").ap()
    recurrent_cells(nc, dram["state_t"], dram["token"], [dram[f"gates{h}"] for h in range(PARTS)], dram["hh"], out_t)
    r = _run(nc, [{f"{n}_dram": a for n, a in arrays.items()}], core_ids=[0])
    return _np.ascontiguousarray(r.results[0]["out_t_dram"].T)
```

```python
import concourse.bass as bass
from concourse import mybir
from contextlib import ExitStack

P = 128
BATCH = 1024
HIDDEN = 256
LAYERS = 6
VOCAB = 4000
KC = HIDDEN // P
QUARTERS = 4
LAST_QUARTER = QUARTERS - 1
QB = BATCH // QUARTERS
TILES = BATCH // P
TPQ = TILES // QUARTERS
PART_LAYERS = [2, 2, 2]
PARTS = len(PART_LAYERS)
FIRST_LAYER = [sum(PART_LAYERS[:h]) for h in range(PARTS)]
STEPS = LAYERS * QUARTERS
LAST_LAYER = STEPS - QUARTERS
GATE_BANKS = 4
WARM_UP = 18

TURN_ORDER = [0, 1, 2, 4, 3, 5, 6, 7] + list(range(8, STEPS))
TURN_OF = {n: k for k, n in enumerate(TURN_ORDER)}
WEIGHTS_AFTER = {1: (0, 0), 2: (0, 5), 3: (1, 0), 4: (1, 2), 5: (1, 4)}
POOL_LOW_STATE = [5, 7, 9, 11, 13, 15, 17, 19]
POOL_LOW_WEIGHTS = [1, 2]


def recurrent_cells(nc, state_t, token, gate_rows, hh, out_t):
    f32, f32r = mybir.dt.float32, mybir.dt.float32r
    i32, u32 = mybir.dt.int32, mybir.dt.uint32
    ALU, ACT = mybir.AluOpType, mybir.ActivationFunctionType

    state_v = state_t.rearrange("(c p) (q b) -> q p c b", p=P, q=QUARTERS)
    out_v = out_t.rearrange("(c p) (q b) -> q p c b", p=P, q=QUARTERS)
    w_v = hh.rearrange("l (c p) n -> l p c n", p=P)

    with ExitStack() as ctx:
        def sb(name, shape, dt):
            return ctx.enter_context(nc.sbuf_tensor(name, shape, dt))

        def sem(name):
            return ctx.enter_context(nc.semaphore(name))

        tok = sb("tok", [P, TILES], i32)
        tok_held = sb("tok_held", [P, TILES], f32)
        wrap = sb("wrap", [P, TILES], f32)
        row_of = sb("row_of", [P, TILES], i32)
        gate = [sb(f"gate{h}", [P, TILES, PART_LAYERS[h] * HIDDEN], f32) for h in range(PARTS)]
        gate_t = sb("gate_t", [P, STEPS, KC, QB], f32)
        w = sb("w", [P, LAYERS, KC, HIDDEN], f32)
        wh = sb("wh", [P, LAYERS, KC, HIDDEN], f32r)
        wl = sb("wl", [P, LAYERS, KC, HIDDEN], f32r)
        s = sb("s", [P, QUARTERS, KC, QB], f32)
        sh = sb("sh", [P, QUARTERS, KC, QB], f32r)
        sl = sb("sl", [P, QUARTERS, KC, QB], f32r)
        pre = sb("pre", [P, QUARTERS, KC, QB], f32)
        ident = sb("ident", [P, P], f32)
        prod = [ctx.enter_context(nc.psum_tensor(f"prod{q}", [P, KC, QB], f32)) for q in range(QUARTERS)]
        turned = [ctx.enter_context(nc.psum_tensor(f"turned{b}", [P, KC, QB], f32)) for b in range(GATE_BANKS)]
        last_prod = [prod[LAST_QUARTER], prod[0]]

        tok_in = sem("tok_in")
        state_in = [sem(f"state_in{q}") for q in range(QUARTERS)]
        w_in = [sem(f"w_in{l}") for l in range(LAYERS)]
        gate_in = [[sem(f"gate_in{h}_{t}") for t in range(TILES)] for h in range(PARTS)]
        ident_zero = sem("ident_zero")
        ident_ready = sem("ident_ready")
        index_step = sem("index_step")
        rows_ready = sem("rows_ready")
        wh_ready = sem("wh_ready")
        wl_dve = sem("wl_dve")
        wl_pool = sem("wl_pool")
        sh_ready = sem("sh_ready")
        sl_dve = sem("sl_dve")
        sl_pool = sem("sl_pool")
        gate_turned = sem("gate_turned")
        gate_ready = sem("gate_ready")
        prod_ready = sem("prod_ready")
        gated = sem("gated")
        pre_ready = sem("pre_ready")
        s_ready = sem("s_ready")
        out_done = sem("out_done")

        def wait_wl(eng, l):
            if l in POOL_LOW_WEIGHTS:
                eng.wait_ge(wl_pool, POOL_LOW_WEIGHTS.index(l) + 1)
            else:
                eng.wait_ge(wl_dve, sum(k not in POOL_LOW_WEIGHTS for k in range(l + 1)))

        def wait_sl(eng, n):
            made = n - QUARTERS
            if made in POOL_LOW_STATE:
                eng.wait_ge(sl_pool, POOL_LOW_STATE.index(made) + 1)
            else:
                eng.wait_ge(sl_dve, n + 1 - sum(k <= made for k in POOL_LOW_STATE))

        with nc.Block() as block:

            @block.sync
            def _(sp):
                def load_state(q):
                    sp.dma_start(s[:, q], state_v[q]).then_inc(state_in[q], 16)

                def load_weights(l):
                    sp.dma_start(w[:, l], w_v[l]).then_inc(w_in[l], 16)

                sp.dma_start(tok[:, :], token).then_inc(tok_in, 16)
                load_state(0)
                load_weights(0)
                load_state(1)
                load_state(2)
                sp.wait_ge(rows_ready, 1)
                load_state(3)
                for l in range(1, LAYERS):
                    h, t = WEIGHTS_AFTER[l]
                    sp.wait_ge(gate_in[h][t], 16)
                    load_weights(l)
                for q in range(QUARTERS - 1):
                    sp.wait_ge(s_ready, LAST_LAYER + q + 1)
                    sp.dma_start(out_v[q], s[:, q]).then_inc(out_done, 16)
                for m in range(KC):
                    sp.wait_ge(s_ready, STEPS + m)
                    sp.dma_start(out_v[LAST_QUARTER][:, m], s[:, LAST_QUARTER, m]).then_inc(out_done, 16)
                sp.wait_ge(out_done, 16 * (QUARTERS - 1 + KC))

            @block.gpsimd
            def _(pool):
                nc.gpsimd.memset(ident[:, :], 0.0).then_inc(ident_zero, 1)
                pool.wait_ge(ident_zero, 1)
                nc.gpsimd.affine_select(out=ident[:, :], in_=ident[:, :], compare_op=ALU.not_equal, fill=1.0,
                                        base=0, pattern=[[-1, P]], channel_multiplier=1).then_inc(ident_ready, 1)

                def gather(h, tiles):
                    for t in tiles:
                        nc.gpsimd.indirect_dma_start(
                            gate[h][:, t], None, gate_rows[h],
                            bass.IndirectOffsetOnAxis(row_of[:, t:t + 1].bitcast(u32), 0),
                        ).then_inc(gate_in[h][t], 16)

                def low_weights(l):
                    pool.wait_ge(w_in[l], 16)
                    pool.wait_ge(wh_ready, l + 1)
                    nc.gpsimd.tensor_tensor(wl[:, l], w[:, l], wh[:, l].bitcast(f32), ALU.subtract).then_inc(wl_pool, 1)

                pool.wait_ge(rows_ready, 1)
                gather(0, range(TILES))
                low_weights(1)
                gather(1, range(5))
                low_weights(2)
                gather(1, range(5, TILES))
                for i, n in enumerate(POOL_LOW_STATE):
                    q = n % QUARTERS
                    pool.wait_ge(s_ready, n + 1)
                    nc.gpsimd.tensor_tensor(sl[:, q], s[:, q], sh[:, q].bitcast(f32), ALU.subtract).then_inc(sl_pool, 1)
                    if i < QUARTERS:
                        gather(2, range(i * TPQ, (i + 1) * TPQ))

            @block.scalar
            def _(act):
                def round_weights(l):
                    act.wait_ge(w_in[l], 16)
                    nc.scalar.copy(wh[:, l], w[:, l]).then_inc(wh_ready, 1)

                def round_input(q):
                    act.wait_ge(state_in[q], 16)
                    nc.scalar.copy(sh[:, q], s[:, q]).then_inc(sh_ready, 1)

                def keep_gates(n):
                    k = TURN_OF[n]
                    act.wait_ge(gate_turned, k + 1)
                    nc.scalar.copy(gate_t[:, n], turned[k % GATE_BANKS][:, :, :]).then_inc(gate_ready, 1)

                def tanh(n):
                    q = n % QUARTERS
                    act.wait_ge(pre_ready, n + 1)
                    if n < LAST_LAYER:
                        nc.scalar.activation(sh[:, q], pre[:, q], ACT.Tanh).then_inc(sh_ready, 1)
                    nc.scalar.activation(s[:, q], pre[:, q], ACT.Tanh).then_inc(s_ready, 1)

                round_input(0)
                round_weights(0)
                for q in range(1, QUARTERS):
                    round_input(q)
                keep_gates(0)
                round_weights(1)
                keep_gates(1)
                tanh(0)
                keep_gates(2)
                keep_gates(4)
                keep_gates(3)
                tanh(1)
                tanh(2)
                round_weights(2)
                tanh(3)
                keep_gates(5)
                keep_gates(6)
                tanh(4)
                keep_gates(7)
                tanh(5)
                keep_gates(8)
                for n in range(6, STEPS - 1):
                    tanh(n)
                    if n + 3 < STEPS:
                        keep_gates(n + 3)
                    if n % QUARTERS == 2 and 3 <= n // QUARTERS + 2 < LAYERS:
                        round_weights(n // QUARTERS + 2)
                for m in range(KC):
                    act.wait_ge(pre_ready, STEPS + m)
                    nc.scalar.activation(s[:, LAST_QUARTER, m], pre[:, LAST_QUARTER, m], ACT.Tanh).then_inc(s_ready, 1)

            @block.vector
            def _(dve):
                dve.wait_ge(tok_in, 16)
                nc.vector.tensor_scalar(tok_held[:, :], tok[:, :], -float(VOCAB), float(VOCAB - 1), ALU.max, ALU.min).then_inc(index_step, 1)
                dve.wait_ge(index_step, 1)
                nc.vector.tensor_scalar(wrap[:, :], tok_held[:, :], 0.0, float(VOCAB), ALU.is_lt, ALU.mult).then_inc(index_step, 1)
                dve.wait_ge(index_step, 2)
                nc.vector.tensor_tensor(row_of[:, :], tok_held[:, :], wrap[:, :], ALU.add).then_inc(rows_ready, 1)

                def low_weights(l):
                    dve.wait_ge(w_in[l], 16)
                    dve.wait_ge(wh_ready, l + 1)
                    nc.vector.tensor_tensor(wl[:, l], w[:, l], wh[:, l].bitcast(f32), ALU.subtract).then_inc(wl_dve, 1)

                def low_state(q):
                    nc.vector.tensor_tensor(sl[:, q], s[:, q], sh[:, q].bitcast(f32), ALU.subtract).then_inc(sl_dve, 1)

                def low_input(q):
                    dve.wait_ge(state_in[q], 16)
                    dve.wait_ge(sh_ready, q + 1)
                    low_state(q)

                low_input(0)
                low_weights(0)
                for q in range(1, QUARTERS):
                    low_input(q)
                for n in range(STEPS - 1):
                    l, q = divmod(n, QUARTERS)
                    dve.wait_ge(prod_ready, n + 1)
                    dve.wait_ge(gate_ready, TURN_OF[n] + 1)
                    nc.vector.tensor_tensor(pre[:, q], prod[q][:, :, :], gate_t[:, n], ALU.mult).then_inc(gated, 1)
                    made = 0 if n == 1 else n - 2
                    if (n == 1 or n >= 3) and made < LAST_LAYER and made not in POOL_LOW_STATE:
                        dve.wait_ge(s_ready, made + 1)
                        low_state(made % QUARTERS)
                    dve.wait_ge(gated, n + 1)
                    nc.vector.tensor_tensor(pre[:, q], pre[:, q], s[:, q], ALU.add).then_inc(pre_ready, 1)
                    if q == 0 and 0 < l < LAYERS - 1 and l + 1 not in POOL_LOW_WEIGHTS:
                        low_weights(l + 1)
                q, n = LAST_QUARTER, STEPS - 1
                dve.wait_ge(gate_ready, STEPS)
                for m in range(KC):
                    dve.wait_ge(prod_ready, STEPS + m)
                    nc.vector.tensor_tensor(pre[:, q, m], last_prod[m][:, m], gate_t[:, n, m], ALU.mult).then_inc(gated, 1)
                for m in range(KC):
                    dve.wait_ge(gated, STEPS + m)
                    nc.vector.tensor_tensor(pre[:, q, m], pre[:, q, m], s[:, q, m], ALU.add).then_inc(pre_ready, 1)

            @block.tensor
            def _(pe):
                def turn(k):
                    n = TURN_ORDER[k]
                    l, q = divmod(n, QUARTERS)
                    h = max(h for h in range(PARTS) if FIRST_LAYER[h] <= l)
                    if k >= GATE_BANKS:
                        pe.wait_ge(gate_ready, k - GATE_BANKS + 1)
                    for t in range(TPQ):
                        tile = q * TPQ + t
                        pe.wait_ge(gate_in[h][tile], 16)
                        for c in range(KC):
                            at = (l - FIRST_LAYER[h]) * HIDDEN + c * P
                            last = nc.tensor.transpose(turned[k % GATE_BANKS][:, c, t * P:(t + 1) * P],
                                                       gate[h][:, tile, at:at + P], ident[:, :])
                    last.then_inc(gate_turned, 1)

                def product(n):
                    l, q = divmod(n, QUARTERS)
                    pe.wait_ge(wh_ready, l + 1)
                    pe.wait_ge(sh_ready, n + 1)
                    for m in range(KC):
                        bank = prod[q] if n < STEPS - 1 else last_prod[m]
                        if n == STEPS - 1 and m == 1:
                            pe.wait_ge(gated, LAST_LAYER + 1)
                        passes = [(wh, sh), (wl, sh), (wh, sl)]
                        for i, (a, b) in enumerate(passes):
                            if m == 0 and i == 1:
                                wait_wl(pe, l)
                            if m == 0 and i == 2:
                                wait_sl(pe, n)
                            for c in range(KC):
                                last = nc.tensor.matmul(bank[:, m, :], a[:, l, c, m * P:(m + 1) * P], b[:, q, c, :],
                                                        start=(i == 0 and c == 0), stop=(i == 2 and c == KC - 1))
                        if m == KC - 1 or n == STEPS - 1:
                            last.then_inc(prod_ready, 1)

                pe.wait_ge(ident_ready, 1)
                for _ in range(WARM_UP):
                    nc.tensor.transpose(turned[0][:, 0, 0:P], ident[:, :], ident[:, :])
                product(0)
                product(1)
                turn(0)
                product(2)
                turn(1)
                product(3)
                turn(2)
                turn(3)
                turn(4)
                product(4)
                turn(5)
                turn(6)
                product(5)
                turn(7)
                product(6)
                turn(8)
                for n in range(7, STEPS):
                    product(n)
                    if n + 2 < STEPS:
                        turn(n + 2)


def kernel(r_state, r_token, L0_rec_ih, L0_rec_hh):
    import numpy as _np
    import concourse.bacc as _bacc
    from concourse import mybir as _mybir
    from concourse.bass_utils import run_bass_kernel_spmd as _run

    ih = _np.asarray(L0_rec_ih).transpose(1, 0, 2)
    arrays = {
        "state_t": _np.ascontiguousarray(_np.asarray(r_state).T),
        "token": _np.ascontiguousarray(_np.asarray(r_token).reshape(TILES, P).T),
        "hh": _np.ascontiguousarray(_np.asarray(L0_rec_hh)),
    }
    for h, l in enumerate(FIRST_LAYER):
        arrays[f"gates{h}"] = _np.ascontiguousarray(ih[:, l:l + PART_LAYERS[h]]).reshape(VOCAB, -1)
    nc = _bacc.Bacc("TRN2", target_bir_lowering=False, num_devices=1)
    dram = {n: nc.dram_tensor(f"{n}_dram", a.shape, _mybir.dt.from_np(a.dtype), kind="ExternalInput").ap() for n, a in arrays.items()}
    out_t = nc.dram_tensor("out_t_dram", (HIDDEN, BATCH), _mybir.dt.float32, kind="ExternalOutput").ap()
    recurrent_cells(nc, dram["state_t"], dram["token"], [dram[f"gates{h}"] for h in range(PARTS)], dram["hh"], out_t)
    r = _run(nc, [{f"{n}_dram": a for n, a in arrays.items()}], core_ids=[0])
    return _np.ascontiguousarray(r.results[0]["out_t_dram"].T)
```
